# Optimizing a Trainium2 kernel written in Bass

```python
import numpy as np
import jax
import jax.numpy as jnp

def _softmax(x, axis=-1):
    return jax.nn.softmax(x, axis=axis)

def _gelu(x):
    return jax.nn.gelu(x, approximate=True)

def _silu(x):
    return jax.nn.silu(x)

def _sigmoid(x):
    return jax.nn.sigmoid(x)

def _layernorm(x, axis=-1, eps=1e-05):
    m = jnp.mean(x, axis=axis, keepdims=True)
    v = jnp.var(x, axis=axis, keepdims=True)
    return (x - m) / jnp.sqrt(v + eps)

def _scatter_add(tgt, idx, src, axis=0):
    return tgt.at[idx].add(src)

def _segment_sum(src, seg, n):
    return jax.ops.segment_sum(src, seg, n)
kernel_name = 'mk_gnn_preln_d1_gnn_r16_5f8bbf'

def setup_inputs(seed: int=0):
    np.random.seed(seed)
    _w = jnp.asarray

    def _rec_inputs():
        import jax
        import jax.numpy as jnp
        _gk = jax.random.key(seed)
        x = -0.0006008 + 1.001 * jax.random.normal(jax.random.fold_in(_gk, 1), (6250, 256), jnp.float32)
        src = jax.random.randint(jax.random.fold_in(_gk, 2), (100000,), 0, 6250, jnp.int32)
        dst = jnp.minimum((6250 * jax.random.uniform(jax.random.fold_in(_gk, 3), (100000,)) ** 2.0).astype(jnp.int32), 99999)
        _o = jnp.argsort(dst, stable=True)
        src = src[_o]
        dst = dst[_o]
        return (x, src, dst)
    x, src, dst = _rec_inputs()

    def _L0_gnn_setup():
        import jax, jax.numpy as jnp
        import numpy as np
        N_NODES = 625
        N_EDGES = 20000
        IN_F, HID_F, OUT_F = (256, 512, 256)

        def _glorot(key, shape):
            lim = np.sqrt(6.0 / (shape[0] + shape[1]))
            return jax.random.uniform(key, shape, jnp.float32, -lim, lim)

        def _sage_mean(h, src, dst, n, deg, W_self, W_neigh, b):
            msum = jax.ops.segment_sum(h[src], dst, num_segments=n)
            h_neigh = msum / jnp.clip(deg, 1.0)[:, None]
            return h @ W_self + h_neigh @ W_neigh + b

        def _sage_pool(h, src, dst, n, deg, W_pool, b_pool, W_self, W_neigh, b):
            hp = jax.nn.relu(h @ W_pool + b_pool)
            hmax = jax.ops.segment_max(hp[src], dst, num_segments=n)
            hmax = jnp.where(deg[:, None] > 0, hmax, 0.0)
            return h @ W_self + hmax @ W_neigh + b

        def _sage_gcn(h, src, dst, n, deg, W_neigh, b):
            msum = jax.ops.segment_sum(h[src], dst, num_segments=n)
            h_neigh = (msum + h) / (deg + 1.0)[:, None]
            return h_neigh @ W_neigh + b
        key = jax.random.key(seed)
        ks = jax.random.split(key, 16)
        inp = {'features': jax.random.normal(ks[0], (N_NODES, IN_F), jnp.float32), 'edge_src': jax.random.randint(ks[1], (N_EDGES,), 0, N_NODES, jnp.int32), 'edge_dst': jax.random.randint(ks[2], (N_EDGES,), 0, N_NODES, jnp.int32), 'W1_self': _glorot(ks[3], (IN_F, HID_F)), 'W1_neigh': _glorot(ks[4], (IN_F, HID_F)), 'b1': jnp.zeros((HID_F,), jnp.float32), 'W2_pool': _glorot(ks[5], (HID_F, HID_F)), 'b2_pool': jnp.zeros((HID_F,), jnp.float32), 'W2_self': _glorot(ks[6], (HID_F, HID_F)), 'W2_neigh': _glorot(ks[7], (HID_F, HID_F)), 'b2': jnp.zeros((HID_F,), jnp.float32), 'W3_neigh': _glorot(ks[8], (HID_F, HID_F)), 'b3': jnp.zeros((HID_F,), jnp.float32), 'W4_self': _glorot(ks[9], (HID_F, HID_F)), 'W4_neigh': _glorot(ks[10], (HID_F, HID_F)), 'b4': jnp.zeros((HID_F,), jnp.float32), 'W_fc': _glorot(ks[11], (HID_F, OUT_F)), 'b_fc': jnp.zeros((OUT_F,), jnp.float32)}
        return inp
    _L0_gnn_all = _L0_gnn_setup()
    _L0_gnn_in = {k: v for k, v in _L0_gnn_all.items() if k in ('W1_self', 'W1_neigh', 'b1', 'W2_pool', 'b2_pool', 'W2_self', 'W2_neigh', 'b2', 'W3_neigh', 'b3', 'W4_self', 'W4_neigh', 'b4', 'W_fc', 'b_fc')}
    del _L0_gnn_all
    return {'x': x, 'src': src, 'dst': dst, 'L0_gnn_W1_self': _L0_gnn_in['W1_self'], 'L0_gnn_W1_neigh': _L0_gnn_in['W1_neigh'], 'L0_gnn_b1': _L0_gnn_in['b1'], 'L0_gnn_W2_pool': _L0_gnn_in['W2_pool'], 'L0_gnn_b2_pool': _L0_gnn_in['b2_pool'], 'L0_gnn_W2_self': _L0_gnn_in['W2_self'], 'L0_gnn_W2_neigh': _L0_gnn_in['W2_neigh'], 'L0_gnn_b2': _L0_gnn_in['b2'], 'L0_gnn_W3_neigh': _L0_gnn_in['W3_neigh'], 'L0_gnn_b3': _L0_gnn_in['b3'], 'L0_gnn_W4_self': _L0_gnn_in['W4_self'], 'L0_gnn_W4_neigh': _L0_gnn_in['W4_neigh'], 'L0_gnn_b4': _L0_gnn_in['b4'], 'L0_gnn_W_fc': _L0_gnn_in['W_fc'], 'L0_gnn_b_fc': _L0_gnn_in['b_fc']}

def reference(x, src, dst, L0_gnn_W1_self, L0_gnn_W1_neigh, L0_gnn_b1, L0_gnn_W2_pool, L0_gnn_b2_pool, L0_gnn_W2_self, L0_gnn_W2_neigh, L0_gnn_b2, L0_gnn_W3_neigh, L0_gnn_b3, L0_gnn_W4_self, L0_gnn_W4_neigh, L0_gnn_b4, L0_gnn_W_fc, L0_gnn_b_fc):
    import jax
    import jax.numpy as jnp

    def _L0_gnn_ref(features, edge_src, edge_dst, W1_self, W1_neigh, b1, W2_pool, b2_pool, W2_self, W2_neigh, b2, W3_neigh, b3, W4_self, W4_neigh, b4, W_fc, b_fc):
        import jax, jax.numpy as jnp
        import numpy as np
        N_NODES = 625
        N_EDGES = 20000
        IN_F, HID_F, OUT_F = (256, 512, 256)

        def _glorot(key, shape):
            lim = np.sqrt(6.0 / (shape[0] + shape[1]))
            return jax.random.uniform(key, shape, jnp.float32, -lim, lim)

        def _sage_mean(h, src, dst, n, deg, W_self, W_neigh, b):
            msum = jax.ops.segment_sum(h[src], dst, num_segments=n)
            h_neigh = msum / jnp.clip(deg, 1.0)[:, None]
            return h @ W_self + h_neigh @ W_neigh + b

        def _sage_pool(h, src, dst, n, deg, W_pool, b_pool, W_self, W_neigh, b):
            hp = jax.nn.relu(h @ W_pool + b_pool)
            hmax = jax.ops.segment_max(hp[src], dst, num_segments=n)
            hmax = jnp.where(deg[:, None] > 0, hmax, 0.0)
            return h @ W_self + hmax @ W_neigh + b

        def _sage_gcn(h, src, dst, n, deg, W_neigh, b):
            msum = jax.ops.segment_sum(h[src], dst, num_segments=n)
            h_neigh = (msum + h) / (deg + 1.0)[:, None]
            return h_neigh @ W_neigh + b
        n = features.shape[0]
        deg = jax.ops.segment_sum(jnp.ones(edge_dst.shape[0], features.dtype), edge_dst, num_segments=n)
        h = _sage_mean(features, edge_src, edge_dst, n, deg, W1_self, W1_neigh, b1)
        h = _sage_pool(h, edge_src, edge_dst, n, deg, W2_pool, b2_pool, W2_self, W2_neigh, b2)
        h = _sage_gcn(h, edge_src, edge_dst, n, deg, W3_neigh, b3)
        h = _sage_mean(h, edge_src, edge_dst, n, deg, W4_self, W4_neigh, b4)
        return h @ W_fc + b_fc
    h = jnp.maximum(_layernorm(x, axis=-1), 0.0)
    x = x + _L0_gnn_ref(h, src, dst, L0_gnn_W1_self, L0_gnn_W1_neigh, L0_gnn_b1, L0_gnn_W2_pool, L0_gnn_b2_pool, L0_gnn_W2_self, L0_gnn_W2_neigh, L0_gnn_b2, L0_gnn_W3_neigh, L0_gnn_b3, L0_gnn_W4_self, L0_gnn_W4_neigh, L0_gnn_b4, L0_gnn_W_fc, L0_gnn_b_fc)
    return x

_drawn_inputs = setup_inputs


def setup_inputs(seed=0):
    import zlib

    import numpy as np

    out = dict(_drawn_inputs(seed))
    spreads = {'L0_gnn_b1': (0.0, 0.1),
     'L0_gnn_b2_pool': (0.0, 0.1),
     'L0_gnn_b2': (0.0, 0.1),
     'L0_gnn_b3': (0.0, 0.1),
     'L0_gnn_b4': (0.0, 0.1),
     'L0_gnn_b_fc': (0.0, 0.1)}
    factors = {}
    for name, (base, spread) in spreads.items():
        noise = np.random.default_rng([zlib.crc32(name.encode()), seed]).standard_normal(out[name].shape)
        drawn = base * np.exp(spread * noise) if base else spread * noise
        out[name] = jnp.asarray(drawn.astype(out[name].dtype))
    for name, factor in factors.items():
        out[name] = (out[name] * factor).astype(out[name].dtype)
    return out
```

```python
from contextlib import ExitStack

import concourse.bass as bass
from concourse import mybir

F32 = mybir.dt.float32
BF16 = mybir.dt.bfloat16
I32 = mybir.dt.int32
ALU = mybir.AluOpType
ACT = mybir.ActivationFunctionType

P = 128
N, IN_F = 6250, 256
HID = 512
E = 100000
COLS = 50
NP_ROWS = N // COLS
ROWS = P * COLS
STEPS = 784
PAD_E = P * STEPS
RING = 16
QUART = RING // 4
LOOPS = STEPS // RING
LAST_E = E - (P - 1) * STEPS
KI, KH = IN_F // P, HID // P
LN_GROUP = 5
EPS = 1e-5
ENDS = 5
V_PADS, V_CLEAR = 2, 10

MEAN1, POOL2, GCN3, MEAN4 = range(4)
WIDTH = [IN_F, HID, HID, IN_F]
COMBINE = [ALU.add, ALU.max, ALU.add, ALU.add]


def gnn(nc, x, src, dst, W1_self, W1_neigh, b1, W2_pool, b2_pool, W2_self, W2_neigh, b2,
        W3_neigh, b3, W4_self, W4_neigh, b4, W_fc, b_fc, out):
    assert NP_ROWS * COLS == N and LOOPS * RING == STEPS and COLS % 2 == 0

    with ExitStack() as ctx:
        def sb(name, shape, dt=F32):
            return ctx.enter_context(nc.sbuf_tensor(name, shape, dt))

        def sem(name):
            return ctx.enter_context(nc.semaphore(name))

        def dram(name, rows, cols):
            return nc.dram_tensor(name, [rows, cols], F32, kind="Internal").ap()

        h_tab = dram("h_tab", ROWS, IN_F)
        mean_tab = dram("mean_tab", ROWS, IN_F)
        hp_self = dram("hp_self", ROWS, HID)
        hp_tab = dram("hp_tab", ROWS, HID)
        u_self = dram("u_self", ROWS, HID)
        u_tab = dram("u_tab", ROWS, HID)
        left_tab = dram("left_tab", ROWS, IN_F)
        right_tab = dram("right_tab", ROWS, IN_F)
        dump = {IN_F: dram("dump256", PAD_E + 1, IN_F), HID: dram("dump512", PAD_E + 1, HID)}
        table = [h_tab, hp_tab, u_tab, right_tab]

        rows = sb("rows", [P, RING, HID])
        state = sb("state", [P, RING, HID])
        src_idx = sb("src_idx", [P, STEPS + RING], I32)
        idx_ring = sb("idx_ring", [P, RING], I32)
        dst_i = sb("dst_i", [P, STEPS], I32)
        dst_f = sb("dst_f", [P, STEPS])
        same = sb("same", [P, STEPS])
        d_hi = sb("d_hi", [P, STEPS])
        d_lo = sb("d_lo", [P, STEPS])
        iota_p = sb("iota_p", [P, P])
        hot_hi = sb("hot_hi", [P, 2, QUART, P], BF16)
        hot_lo = sb("hot_lo", [P, 2, QUART, COLS], BF16)
        ident = sb("ident", [P, P])
        lower = sb("lower", [P, P])
        ones = sb("ones", [P, P])
        part_base = sb("part_base", [P, 1])
        first_cnt = sb("first_cnt", [P, 1])
        fix_idx = sb("fix_idx", [P, 1], I32)
        ends_row = sb("ends_row", [P, 2, P])
        ends_col = sb("ends_col", [P, 2, P])
        cross = sb("cross", [P, P])
        carry_m = sb("carry_m", [P, P])
        tails = sb("tails", [P, KH, P])
        carry = sb("carry", [P, KH, P])
        fix_row = rows[:, RING - 2, :]
        fix_out = rows[:, RING - 1, :]
        deg = sb("deg", [P, COLS])
        deg_cum = sb("deg_cum", [P, COLS])
        deg_off = sb("deg_off", [P, 1])
        deg_tmp = sb("deg_tmp", [P, COLS])
        has_in = sb("has_in", [P, COLS])
        r_mean = sb("r_mean", [P, COLS])
        r_gcn = sb("r_gcn", [P, COLS])
        end_idx = sb("end_idx", [P, COLS + ENDS], I32)
        zero_row = sb("zero_row", [1, HID])
        ln_stat = sb("ln_stat", [P, LN_GROUP, 6])
        ln_mv = sb("ln_mv", [P, LN_GROUP, 2])
        ln_rstd = sb("ln_rstd", [P, LN_GROUP])
        ln_sd = sb("ln_sd", [P, LN_GROUP])
        ln_bias = sb("ln_bias", [P, LN_GROUP])
        eps_col = sb("eps_col", [P, 1])
        w_raw = sb("w_raw", [P, KH, HID])
        w_t = sb("w_t", [P, KH, HID])
        w2p = sb("w2p", [P, KH, HID])
        wfc = sb("wfc", [P, KH, IN_F])
        A1 = sb("A1", [P, KI, HID])
        A2 = sb("A2", [P, KI, HID])
        PQ = sb("PQ", [P, KH, HID])
        R = w2p
        B1 = sb("B1", [P, KH, HID])
        B2 = sb("B2", [P, KH, HID])
        C1 = sb("C1", [P, KI, HID])
        C2 = sb("C2", [P, KI, HID])
        bcol = sb("bcol", [P, 4, KH])
        brow = sb("brow", [1, 2, HID])
        bias_hp = sb("bias_hp", [1, HID])
        bias_u = sb("bias_u", [1, HID])
        bias_v = sb("bias_v", [P, HID])
        side_in = sb("side_in", [P, 2, HID])
        side_t = sb("side_t", [P, 2, KH, P])
        side_out = sb("side_out", [P, 2, HID])
        end_ring = sb("end_ring", [P, ENDS], I32)
        ends = rows[:, 0:ENDS, :]
        add_in = sb("add_in", [P, 2, HID])
        ends_t = sb("ends_t", [P, 2, KH, P])
        scaled = sb("scaled", [P, 2, HID])
        done = sb("done", [P, 2, HID])

        x_in = sb("x_in", [P, 2, IN_F])
        iota_i = sb("iota_i", [P, P], I32)
        base_i = sb("base_i", [P, 1], I32)
        bias_vr = bias_hp
        psum = [ctx.enter_context(nc.psum_tensor(f"psum{i}", [P, HID], F32)) for i in range(8)]

        s_init = sem("constants_set")
        s_mask = sem("constants_masked")
        s_idx_in = sem("edges_loaded")
        s_w_in = sem("shared_weights_loaded")
        s_v = sem("vector_chain")
        s_x = [sem(f"x_loaded{i}") for i in range(2)]
        s_bn = sem("ln_chain")
        s_vopen = sem("ln_groups")
        s_lnstat = sem("ln_stats_ready")
        s_lnsd = sem("ln_sd_ready")
        s_lnscale = sem("ln_scale_ready")
        s_h = sem("h_ready")
        s_hst = [sem(f"h_stored{i}") for i in range(2)]
        s_ecol = sem("edge_columns_ready")
        s_erow = sem("edge_rows_ready")
        s_ring = sem("indices_ready")
        s_row = [sem(f"row_in{i}") for i in range(RING)]
        s_open = sem("gather_quarters")
        s_state = sem("state_done")
        s_dump = [sem(f"state_dumped{i}") for i in range(4)]
        s_hot = sem("onehots_ready")
        s_hist = sem("onehots_counted")
        s_dtot = sem("degree_totals_ready")
        s_doff = sem("degree_offsets_ready")
        s_deg = sem("end_indices_ready")
        s_fixT = sem("tails_transposed")
        s_carry = sem("carries_ready")
        s_carryT = sem("carries_transposed")
        s_fixin = sem("boundary_rows_in")
        s_fixout = sem("boundary_rows_fixed")
        s_fixed = sem("boundary_rows_stored")
        s_wx = sem("weight_loaded")
        s_wT = sem("weight_transposed")
        s_wTc = sem("weight_transpose_copied")
        s_wmm = sem("weight_product_ready")
        s_woc = sem("weight_product_copied")
        s_sin = [sem(f"side_loaded{i}") for i in range(2)]
        s_sT = sem("side_transposed")
        s_sTc = sem("side_transpose_copied")
        s_smm = sem("side_product_ready")
        s_soc = sem("side_product_copied")
        s_sst = [sem(f"side_stored{i}") for i in range(2)]
        s_eidx = sem("end_ring_ready")
        s_ein = [sem(f"ends_in{i}") for i in range(ENDS)]
        s_add = [sem(f"addend_loaded{i}") for i in range(2)]
        s_sc = sem("tile_scaled")
        s_tT = sem("tile_transposed")
        s_tTc = sem("tile_transpose_copied")
        s_tmm = sem("tile_product_ready")
        s_sum = sem("tile_summed")
        s_relu = sem("tile_relu_done")
        s_mst = [sem(f"mean_stored{i}") for i in range(2)]
        s_tst = [sem(f"tile_stored{i}") for i in range(2)]
        s_zero = sem("zero_rows_stored")
        s_out = [sem(f"out_stored{i}") for i in range(2)]

        x_v = x.rearrange("(p t) f -> p t f", t=COLS)
        out_v = out.rearrange("(p t) f -> p t f", t=COLS)
        tiles = {id(t): t.rearrange("(p t) f -> p t f", t=COLS)
                 for t in (h_tab, mean_tab, hp_self, hp_tab, u_self, u_tab, left_tab, right_tab)}
        dump_v = {w: dump[w][0:PAD_E, :].rearrange("(p j) w -> p j w", p=P) for w in dump}
        rows_flat = rows[:, :, :].rearrange("p r w -> p (r w)")
        state_flat = state[:, :, :].rearrange("p r w -> p (r w)")

        def ln_x(b):
            return rows_flat[:, b * LN_GROUP * IN_F:(b + 1) * LN_GROUP * IN_F].rearrange(
                "p (t f) -> p t f", f=IN_F)

        def ln_h(b):
            return state_flat[:, b * LN_GROUP * IN_F:(b + 1) * LN_GROUP * IN_F].rearrange(
                "p (t f) -> p t f", f=IN_F)

        def cols(ap, t, n=1):
            return ap[:, bass.ds(t, n)]

        def node_tile(ap, t):
            return tiles[id(ap)][:, bass.ds(t, 1), :].rearrange("p t f -> p (t f)")

        def ein_value(k, i, n):
            return (k * (COLS // ENDS) + 2 * i + n // ENDS + 1) * 16

        EARLY = [(W1_self, KI, w2p, 0, HID, A1), (W1_neigh, KI, w2p, 0, HID, A2)]
        LATE = [(W4_self, KH, wfc, 0, IN_F, PQ), (W4_neigh, KH, wfc, IN_F, IN_F, PQ),
                (W3_neigh, KH, PQ, 0, HID, R), (W2_self, KH, R, 0, HID, B1),
                (W2_neigh, KH, R, 0, HID, B2), (W1_self, KI, B1, 0, HID, C1),
                (W1_neigh, KI, B1, 0, HID, C2)]
        PRODUCTS = EARLY + LATE
        N_EARLY_OUT = sum(p[1] for p in EARLY)
        N_OUT = sum(p[1] for p in PRODUCTS)

        block = ctx.enter_context(nc.Block())

        @block.gpsimd
        def _(pool):
            nc.gpsimd.memset(ident[:, :], 0.0).then_inc(s_init, 1)
            nc.gpsimd.memset(ones[:, :], 1.0).then_inc(s_init, 1)
            nc.gpsimd.memset(zero_row[:, :], 0.0).then_inc(s_init, 1)
            nc.gpsimd.iota(iota_i[:, :], pattern=[[1, P]], base=0, channel_multiplier=0).then_inc(s_init, 1)
            nc.gpsimd.iota(base_i[:, :], pattern=[[0, 1]], base=0, channel_multiplier=STEPS).then_inc(s_init, 1)
            pool.wait_ge(s_init, 5)
            nc.gpsimd.affine_select(out=ident[:, :], in_=ident[:, :], compare_op=ALU.not_equal, fill=1.0,
                                    base=0, pattern=[[-1, P]], channel_multiplier=1).then_inc(s_mask, 1)
            nc.gpsimd.affine_select(out=lower[:, :], in_=ones[:, :], compare_op=ALU.is_gt, fill=0.0,
                                    base=0, pattern=[[1, P]], channel_multiplier=-1).then_inc(s_mask, 1)

            def gathers(k):
                def body(i, first):
                    for q in range(4):
                        pool.wait_ge(s_ring, (k * LOOPS + i) * 4 + q + 1)
                        pool.sem_inc(s_open)
                        for u in range(q * QUART, (q + 1) * QUART):
                            nc.gpsimd.indirect_dma_start(
                                out=rows[:, u, 0:WIDTH[k]], out_offset=None, in_=table[k],
                                in_offset=bass.IndirectOffsetOnAxis(ap=idx_ring[:, u:u + 1], axis=0),
                            ).then_inc(s_row[u], 16)

                body(0, True)
                with pool.Fori(1, LOOPS) as i:
                    body(i, False)

            def fix_boundaries(k):
                w = WIDTH[k]
                for q in range(4):
                    pool.wait_ge(s_dump[q], 16 * LOOPS * (k + 1))
                if k == 0:
                    pool.wait_ge(s_deg, 1)
                nc.gpsimd.indirect_dma_start(
                    out=fix_row[:, 0:w], out_offset=None, in_=dump[w],
                    in_offset=bass.IndirectOffsetOnAxis(ap=fix_idx[:, 0:1], axis=0)).then_inc(s_fixin, 16)
                pool.wait_ge(s_fixout, k + 1)
                nc.gpsimd.indirect_dma_start(
                    out=dump[w], out_offset=bass.IndirectOffsetOnAxis(ap=fix_idx[:, 0:1], axis=0),
                    in_=fix_out[:, 0:w], in_offset=None).then_inc(s_fixed, 16)
                pool.wait_ge(s_fixed, 16 * (k + 1))

            def gather_ends(k):
                w = WIDTH[k]

                def body(i, first):
                    for r in range(ENDS):
                        pool.wait_ge(s_eidx, k * COLS + i * ENDS + r + 1)
                        pool.sem_inc(s_open)
                        nc.gpsimd.indirect_dma_start(
                            out=ends[:, r, 0:w], out_offset=None, in_=dump[w],
                            in_offset=bass.IndirectOffsetOnAxis(ap=end_ring[:, r:r + 1], axis=0),
                        ).then_inc(s_ein[r], 16)

                if k == 0:
                    pool.wait_ge(s_zero, 32)
                body(0, True)
                with pool.Fori(1, COLS // ENDS) as i:
                    body(i, False)

            for b in range(2):
                pool.wait_ge(s_hst[b], 16 * (COLS // LN_GROUP // 2))
            for k in (MEAN1, POOL2, GCN3, MEAN4):
                if k == POOL2:
                    for b in range(2):
                        pool.wait_ge(s_tst[b], 16 * COLS // 2)
                if k == GCN3:
                    for b in range(2):
                        pool.wait_ge(s_tst[b], 16 * COLS)
                if k == MEAN4:
                    for b in range(2):
                        pool.wait_ge(s_tst[b], 16 * COLS + 32 * COLS // 2)
                gathers(k)
                fix_boundaries(k)
                gather_ends(k)

        @block.sync
        def _(sp):
            sp.wait_ge(s_v, V_PADS)
            for t, d in ((src, src_idx), (dst, dst_i)):
                whole = t[0:(P - 1) * STEPS].rearrange("(p j) -> p j", j=STEPS)
                sp.dma_start(d[0:112, 0:STEPS], whole[0:112, :]).then_inc(s_idx_in, 16)
                sp.dma_start(d[112:P - 1, 0:STEPS], whole[112:P - 1, :]).then_inc(s_idx_in, 16)
                sp.dma_start(d[P - 1:P, 0:LAST_E],
                             t[(P - 1) * STEPS:E].rearrange("(a n) -> a n", a=1)).then_inc(s_idx_in, 16)

            def load_x(i, b):
                g = 2 * i + b
                for p0, p1 in ((0, 112), (112, NP_ROWS)):
                    sp.dma_start(ln_x(b)[p0:p1, :, :],
                                 x_v[p0:p1, bass.ds(g * LN_GROUP, LN_GROUP), :]).then_inc(s_x[b], 16)

            def store_h(i, b):
                g = 2 * i + b
                sp.wait_ge(s_h, g + 1)
                sp.dma_start(tiles[id(h_tab)][:, bass.ds(g * LN_GROUP, LN_GROUP), :],
                             ln_h(b)).then_inc(s_hst[b], 16)

            sp.wait_ge(s_v, V_CLEAR)
            for b in range(2):
                load_x(0, b)
            sp.dma_start(w2p[:, :, :], W2_pool.rearrange("(c p) n -> p c n", p=P)).then_inc(s_w_in, 16)
            sp.dma_start(wfc[:, :, :], W_fc.rearrange("(c p) n -> p c n", p=P)).then_inc(s_w_in, 16)
            with nc.allow_non_contiguous_dma(reason="four bias vectors of 512"):
                for n, b in enumerate((b1, b2, b3, b4)):
                    sp.dma_start(bcol[:, n, :], b.rearrange("(c p) -> p c", p=P)).then_inc(s_w_in, 16)
            sp.dma_start(brow[0:1, 0, :], b2_pool.rearrange("(a n) -> a n", a=1)).then_inc(s_w_in, 16)
            sp.dma_start(brow[0:1, 1, 0:IN_F], b_fc.rearrange("(a n) -> a n", a=1)).then_inc(s_w_in, 16)
            sp.wait_ge(s_init, 5)
            for w in (IN_F, HID):
                sp.dma_start(dump[w][PAD_E:PAD_E + 1, :], zero_row[:, 0:w]).then_inc(s_zero, 16)
            with sp.Fori(1, COLS // LN_GROUP // 2) as i:
                for b in range(2):
                    store_h(i - 1, b)
                    load_x(i, b)
            for b in range(2):
                store_h(COLS // LN_GROUP // 2 - 1, b)

            def dumps(k):
                w = WIDTH[k]

                def body(i):
                    for q in range(4):
                        sp.wait_ge(s_state, k * STEPS + i * RING + (q + 1) * QUART)
                        sp.dma_start(dump_v[w][:, bass.ds(i * RING + q * QUART, QUART), :],
                                     state[:, q * QUART:(q + 1) * QUART, 0:w]).then_inc(s_dump[q], 16)

                body(0)
                with sp.Fori(1, LOOPS) as i:
                    body(i)

            def finish(k, addend, stores):
                base = [0, 0, 1, 2][k] * COLS // 2 if k != GCN3 else 0

                def load(t, s):
                    node, add_slot, width = addend
                    sp.dma_start(add_in[:, s, 0:width], node_tile(node, t)).then_inc(s_add[s], 16)
                    if k == MEAN4:
                        sp.dma_start(x_in[0:NP_ROWS, s, :],
                                     x_v[:, bass.ds(t, 1), :].rearrange("p t f -> p (t f)")).then_inc(s_add[s], 16)

                def store(t, s):
                    if k == MEAN1:
                        sp.wait_ge(s_sc, t + 1)
                        sp.dma_start(node_tile(mean_tab, t), scaled[:, s, 0:IN_F]).then_inc(s_mst[s], 16)
                        sp.wait_ge(s_relu, t + 1)
                        sp.dma_start(node_tile(hp_tab, t), done[:, s, :]).then_inc(s_tst[s], 16)
                    elif k == POOL2:
                        sp.wait_ge(s_sum, COLS + t + 1)
                        sp.dma_start(node_tile(u_tab, t), done[:, s, :]).then_inc(s_tst[s], 16)
                    elif k == GCN3:
                        sp.wait_ge(s_sum, 2 * COLS + t + 1)
                        sp.dma_start(node_tile(left_tab, t), done[:, s, 0:IN_F]).then_inc(s_tst[s], 16)
                        sp.dma_start(node_tile(right_tab, t), done[:, s, IN_F:HID]).then_inc(s_tst[s], 16)
                    else:
                        sp.wait_ge(s_sum, 3 * COLS + t + 1)
                        sp.dma_start(out_v[:, bass.ds(t, 1), :].rearrange("p t f -> p (t f)"),
                                     done[0:NP_ROWS, s, 0:IN_F]).then_inc(s_out[s], 16)

                if k == MEAN1:
                    sp.wait_ge(s_sst[0], 16 * COLS)
                if k == POOL2:
                    sp.wait_ge(s_sst[0], 16 * COLS + 8 * COLS)
                    sp.wait_ge(s_sst[1], 8 * COLS)
                if k == MEAN4:
                    for s in range(2):
                        sp.wait_ge(s_tst[s], 16 * COLS + 32 * COLS // 2)
                for s in range(2):
                    load(s, s)
                with sp.Fori(1, COLS // 2) as i:
                    for s in range(2):
                        store(2 * i - 2 + s, s)
                        load(2 * i + s, s)
                for s in range(2):
                    store(COLS - 2 + s, s)

            dumps(MEAN1)
            finish(MEAN1, (hp_self, None, HID), None)
            dumps(POOL2)
            finish(POOL2, (u_self, None, HID), None)
            dumps(GCN3)
            finish(GCN3, (u_tab, None, HID), None)
            dumps(MEAN4)
            finish(MEAN4, (left_tab, None, IN_F), None)
            for s in range(2):
                sp.wait_ge(s_out[s], 16 * COLS // 2)

        @block.scalar
        def _(act):
            copied = [0, 0]

            def load_factor(n):
                w, chunks = PRODUCTS[n][0:2]
                if n:
                    act.wait_ge(s_wT, KH * n)
                act.dma_start(w_raw[:, 0:chunks, :], w.rearrange("(c p) n -> p c n", p=P)).then_inc(s_wx, 16)

            def product(n):
                w, chunks, right, c0, width, result = PRODUCTS[n]
                for m in range(KH):
                    act.wait_ge(s_wT, KH * n + m + 1)
                    if n and m == 0:
                        act.wait_ge(s_wmm, copied[1])
                    nc.scalar.activation(w_t[:, m, 0:chunks * P], psum[m % 2][:, 0:chunks * P],
                                         ACT.Copy).then_inc(s_wTc, 1)
                if n + 1 < len(PRODUCTS) and n + 1 != len(EARLY):
                    load_factor(n + 1)
                for c in range(chunks):
                    act.wait_ge(s_wmm, copied[1] + 1)
                    nc.scalar.activation(result[:, c, c0:c0 + width], psum[2 + c % 2][:, 0:width],
                                         ACT.Copy).then_inc(s_woc, 1)
                    copied[1] += 1

            load_factor(0)

            def normalise(i, b, first):
                g = 2 * i + b
                act.wait_ge(s_lnstat, g + 1)
                if not (first and b == 0):
                    act.wait_ge(s_lnscale, g)
                nc.scalar.activation(ln_sd[:, :], ln_mv[:, :, 1:2].rearrange("p t a -> p (t a)"),
                                     ACT.Sqrt, bias=eps_col[:, 0:1]).then_inc(s_lnsd, 1)
                act.wait_ge(s_lnscale, g + 1)
                if not first:
                    act.wait_ge(s_hst[b], 16 * i)
                for t in range(LN_GROUP):
                    ins = nc.scalar.activation(ln_h(b)[:, t, :], ln_x(b)[:, t, :], ACT.Relu,
                                               bias=ln_bias[:, t:t + 1], scale=ln_rstd[:, t:t + 1])
                ins.then_inc(s_h, 1)

            for b in range(2):
                normalise(0, b, True)
            with act.Fori(1, COLS // LN_GROUP // 2) as i:
                for b in range(2):
                    normalise(i, b, False)
            for n in range(len(EARLY)):
                product(n)
            act.wait_ge(s_wmm, N_EARLY_OUT + 1)
            nc.scalar.activation(bias_hp[:, :], psum[2][0:1, :], ACT.Copy).then_inc(s_woc, 1)
            copied[1] += 1
            load_factor(len(EARLY))

            def side_hp(t, first):
                if not first:
                    act.wait_ge(s_sT, t)
                act.dma_start(side_in[:, 0, 0:IN_F], node_tile(h_tab, t)).then_inc(s_sin[0], 16)
                act.wait_ge(s_sT, t + 1)
                if not first:
                    act.wait_ge(s_smm, t)
                nc.scalar.activation(side_t[:, 0, 0:KI, :].rearrange("p a b -> p (a b)"),
                                     psum[0][:, 0:IN_F], ACT.Copy).then_inc(s_sTc, 1)
                act.wait_ge(s_smm, t + 1)
                if not first:
                    act.wait_ge(s_sst[0], 16 * t)
                nc.scalar.activation(side_out[:, 0, :], psum[2][:, :], ACT.Copy).then_inc(s_soc, 1)
                act.wait_ge(s_soc, t + 1)
                act.dma_start(node_tile(hp_self, t), side_out[:, 0, :]).then_inc(s_sst[0], 16)

            for b in range(2):
                act.wait_ge(s_hst[b], 16 * (COLS // LN_GROUP // 2))
            side_hp(0, True)
            with act.Fori(1, COLS) as t:
                side_hp(t, False)

            def tile_copies(k):
                chunks = WIDTH[k] // P
                base = (k - MEAN1) * COLS

                def transposed(t, s, first):
                    act.wait_ge(s_tT, base + t + 1)
                    if not first:
                        act.wait_ge(s_tmm, base + t - 1)
                    nc.scalar.activation(ends_t[:, s, 0:chunks, :].rearrange("p a b -> p (a b)"),
                                         psum[4 + s][:, 0:chunks * P], ACT.Copy).then_inc(s_tTc, 1)

                def relu(t, s):
                    act.wait_ge(s_sum, t + 1)
                    nc.scalar.activation(done[:, s, :], done[:, s, :], ACT.Relu).then_inc(s_relu, 1)

                transposed(0, 0, True)
                transposed(1, 1, True)
                if k == MEAN1:
                    relu(0, 0)
                with act.Fori(1, COLS // 2) as i:
                    transposed(2 * i, 0, False)
                    if k == MEAN1:
                        relu(2 * i - 1, 1)
                    transposed(2 * i + 1, 1, False)
                    if k == MEAN1:
                        relu(2 * i, 0)
                if k == MEAN1:
                    relu(COLS - 1, 1)

            tile_copies(MEAN1)

            for n in range(len(EARLY), len(PRODUCTS)):
                product(n)
            for row, bank in ((bias_u, 3), (bias_vr, 2)):
                act.wait_ge(s_wmm, copied[1] + 1)
                nc.scalar.activation(row[:, :], psum[bank][0:1, :],
                                     ACT.Copy).then_inc(s_woc, 1)
                copied[1] += 1
            act.wait_ge(s_wmm, copied[1] + 1)
            nc.scalar.activation(bias_v[:, :], psum[2][:, :], ACT.Copy).then_inc(s_woc, 1)
            copied[1] += 1

            def load_side(t, s):
                act.dma_start(side_in[:, s, 0:IN_F], node_tile(h_tab, t)).then_inc(s_sin[s], 16)
                act.dma_start(side_in[:, s, IN_F:HID], node_tile(mean_tab, t)).then_inc(s_sin[s], 16)

            def side_u(t, s, first, last):
                act.wait_ge(s_sT, COLS + t + 1)
                if not first:
                    act.wait_ge(s_smm, COLS + t - 1)
                nc.scalar.activation(side_t[:, s, :, :].rearrange("p a b -> p (a b)"),
                                     psum[s][:, :], ACT.Copy).then_inc(s_sTc, 1)
                if not last:
                    load_side(t + 2, s)
                act.wait_ge(s_smm, COLS + t + 1)
                if s == 0 or not first:
                    act.wait_ge(s_sst[s], 16 * COLS + 8 * t if s == 0 else 8 * (t - 1))
                nc.scalar.activation(side_out[:, s, :], psum[2 + s][:, :], ACT.Copy).then_inc(s_soc, 1)
                act.wait_ge(s_soc, COLS + t + 1)
                act.dma_start(node_tile(u_self, t), side_out[:, s, :]).then_inc(s_sst[s], 16)

            for s in range(2):
                act.wait_ge(s_mst[s], 16 * COLS // 2)
            for s in range(2):
                load_side(s, s)
            for s in range(2):
                side_u(s, s, True, False)
            with act.Fori(1, COLS // 2 - 1) as i:
                for s in range(2):
                    side_u(2 * i + s, s, False, False)
            for s in range(2):
                side_u(COLS - 2 + s, s, False, True)
            tile_copies(POOL2)

        @block.tensor
        def _(pe):
            outs = [0]

            def product(n):
                w, chunks, right, c0, width, result = PRODUCTS[n]
                pe.wait_ge(s_wx, 16 * (n + 1))
                for m in range(KH):
                    if KH * n + m >= 2:
                        pe.wait_ge(s_wTc, KH * n + m - 1)
                    for c in range(chunks):
                        ins = nc.tensor.transpose(psum[m % 2][:, c * P:(c + 1) * P],
                                                  w_raw[:, c, m * P:(m + 1) * P], ident[:, :])
                    ins.then_inc(s_wT, 1)
                pe.wait_ge(s_wTc, KH * (n + 1))
                pe.wait_ge(s_woc, outs[0])
                for c in range(chunks):
                    if c >= 2:
                        pe.wait_ge(s_woc, outs[0] - 1)
                    for m in range(KH):
                        ins = nc.tensor.matmul(psum[2 + c % 2][:, 0:width], w_t[:, m, c * P:(c + 1) * P],
                                               right[:, m, 0:width], start=(m == 0), stop=(m == KH - 1))
                    ins.then_inc(s_wmm, 1)
                    outs[0] += 1

            def bias_row(bank, terms):
                pe.wait_ge(s_woc, outs[0])
                for n, (left, right) in enumerate(terms):
                    ins = nc.tensor.matmul(psum[bank][0:1, 0:right.shape[-1]], left, right,
                                           start=(n == 0), stop=(n == len(terms) - 1))
                ins.then_inc(s_wmm, 1)
                outs[0] += 1

            def by_chunks(n, right):
                return [(bcol[:, n, c:c + 1], right[:, c, :]) for c in range(KH)]

            pe.wait_ge(s_mask, 2)
            pe.wait_ge(s_ecol, 1)
            for n in range(2):
                ins = nc.tensor.transpose(psum[5][:, n * P:(n + 1) * P], ends_col[:, n, :], ident[:, :])
            ins.then_inc(s_erow, 1)
            pe.wait_ge(s_w_in, 16 * 8)
            for n in range(len(EARLY)):
                product(n)
            one = ones[0:1, 0:1]
            bias_row(2, by_chunks(0, w2p) + [(one, brow[0:1, 0, :])])
            pe.wait_ge(s_woc, outs[0])

            def count(i, q, first):
                pe.wait_ge(s_hot, 4 * i + q + 1)
                for n in range(QUART):
                    ins = nc.tensor.matmul(psum[7][:, 0:COLS], hot_hi[:, q % 2, n, :], hot_lo[:, q % 2, n, :],
                                           start=(first and q == 0 and n == 0), stop=False,
                                           skip_group_check=True)
                ins.then_inc(s_hist, 1)

            def side_hp_transposes(t, first):
                pe.wait_ge(s_sin[0], 16 * (t + 1))
                if not first:
                    pe.wait_ge(s_sTc, t)
                for c in range(KI):
                    ins = nc.tensor.transpose(psum[0][:, c * P:(c + 1) * P],
                                              side_in[:, 0, c * P:(c + 1) * P], ident[:, :])
                ins.then_inc(s_sT, 1)

            def side_hp_product(t, first):
                pe.wait_ge(s_sTc, t + 1)
                if not first:
                    pe.wait_ge(s_soc, t)
                nc.tensor.matmul(psum[2][:, :], ones[0:1, :], bias_hp[:, :], start=True, stop=False)
                for c in range(KI):
                    ins = nc.tensor.matmul(psum[2][:, :], side_t[:, 0, c, :], A1[:, c, :],
                                           start=False, stop=(c == KI - 1))
                ins.then_inc(s_smm, 1)

            def pass1(i, first):
                count(i, 0, first)
                side_hp_transposes(i, first)
                count(i, 1, first)
                count(i, 2, first)
                side_hp_product(i, first)
                count(i, 3, first)

            pass1(0, True)
            with pe.Fori(1, LOOPS) as i:
                pass1(i, False)
            for t in range(LOOPS, COLS):
                side_hp_transposes(t, False)
                side_hp_product(t, False)
            pe.wait_ge(s_dtot, 1)
            nc.tensor.matmul(psum[6][:, 0:1], lower[:, :], deg_cum[:, COLS - 1:COLS],
                             start=True, stop=True).then_inc(s_doff, 1)

            def fix_boundaries(k):
                chunks = WIDTH[k] // P
                pe.wait_ge(s_state, (k + 1) * STEPS)
                if k:
                    pe.wait_ge(s_tTc, min(k, 2) * COLS)
                for c in range(chunks):
                    ins = nc.tensor.transpose(psum[4][:, c * P:(c + 1) * P],
                                              state[:, RING - 1, c * P:(c + 1) * P], ident[:, :])
                ins.then_inc(s_fixT, 1)
                pe.wait_ge(s_carry, k + 1)
                for c in range(chunks):
                    ins = nc.tensor.transpose(psum[5][:, c * P:(c + 1) * P], carry[:, c, :], ident[:, :])
                ins.then_inc(s_carryT, 1)

            def tile_products(k, right):
                chunks = WIDTH[k] // P
                base = (k - MEAN1) * COLS

                def transposes(i, n, first):
                    t, s, r = i * 2 * ENDS + n, n % 2, n % ENDS
                    if k == MEAN1:
                        pe.wait_ge(s_sc, t + 1)
                        source = scaled[:, s, 0:IN_F]
                    else:
                        pe.wait_ge(s_ein[r], ein_value(k, i, n))
                        source = ends[:, r, :]
                    if not first:
                        pe.wait_ge(s_tTc, base + t - 1)
                    for c in range(chunks):
                        ins = nc.tensor.transpose(psum[4 + s][:, c * P:(c + 1) * P],
                                                  source[:, c * P:(c + 1) * P], ident[:, :])
                    ins.then_inc(s_tT, 1)

                def products(t, s, first):
                    pe.wait_ge(s_tTc, base + t + 1)
                    if not first:
                        pe.wait_ge(s_sum, base + t - 1)
                    for c in range(chunks):
                        ins = nc.tensor.matmul(psum[6 + s][:, :], ends_t[:, s, c, :], right[:, c, :],
                                               start=(c == 0), stop=(c == chunks - 1))
                    ins.then_inc(s_tmm, 1)

                pe.wait_ge(s_fixout, k + 1)
                if k == MEAN1:
                    pe.wait_ge(s_deg, 1)
                def body(i, first):
                    for t in range(2 * ENDS):
                        transposes(i, t, first and t < 2)
                        if not (first and t == 0):
                            products(i * 2 * ENDS + t - 1, (t - 1) % 2, first and t < 3)

                body(0, True)
                with pe.Fori(1, COLS // (2 * ENDS)) as i:
                    body(i, False)
                products(COLS - 1, 1, False)

            fix_boundaries(MEAN1)
            tile_products(MEAN1, A2)

            for n in range(len(EARLY), len(PRODUCTS)):
                product(n)
            bias_row(3, by_chunks(1, R) + by_chunks(0, B1))
            bias_row(2, by_chunks(2, PQ) + [(one, brow[0:1, 1, :])] + by_chunks(3, wfc))
            pe.wait_ge(s_woc, outs[0])
            nc.tensor.matmul(psum[2][:, :], ones[0:1, :], bias_vr[:, :], start=True, stop=True).then_inc(s_wmm, 1)
            outs[0] += 1
            pe.wait_ge(s_woc, outs[0])

            def side_u_transposes(t, s, first):
                pe.wait_ge(s_sin[s], 16 * COLS + 16 * (t + 2) if s == 0 else 16 * (t + 1))
                if not first:
                    pe.wait_ge(s_sTc, COLS + t - 1)
                for c in range(KH):
                    ins = nc.tensor.transpose(psum[s][:, c * P:(c + 1) * P],
                                              side_in[:, s, c * P:(c + 1) * P], ident[:, :])
                ins.then_inc(s_sT, 1)

            def side_u_product(t, s, first):
                pe.wait_ge(s_sTc, COLS + t + 1)
                if not first:
                    pe.wait_ge(s_soc, COLS + t - 1)
                nc.tensor.matmul(psum[2 + s][:, :], ones[0:1, :], bias_u[:, :], start=True, stop=False)
                for c in range(KH):
                    right = (C1 if c < KI else C2)[:, c % KI, :]
                    ins = nc.tensor.matmul(psum[2 + s][:, :], side_t[:, s, c, :], right,
                                           start=False, stop=(c == KH - 1))
                ins.then_inc(s_smm, 1)

            side_u_transposes(0, 0, True)
            side_u_transposes(1, 1, True)
            side_u_product(0, 0, True)
            side_u_transposes(2, 0, False)
            side_u_product(1, 1, True)
            with pe.Fori(1, COLS // 2 - 1) as i:
                side_u_transposes(2 * i + 1, 1, False)
                side_u_product(2 * i, 0, False)
                side_u_transposes(2 * i + 2, 0, False)
                side_u_product(2 * i + 1, 1, False)
            side_u_transposes(COLS - 1, 1, False)
            side_u_product(COLS - 2, 0, False)
            side_u_product(COLS - 1, 1, False)

            fix_boundaries(POOL2)
            tile_products(POOL2, B2)
            fix_boundaries(GCN3)
            fix_boundaries(MEAN4)

        @block.vector
        def _(dve):
            chain = [0]

            def link(ins):
                chain[0] += 1
                ins.then_inc(s_v, 1)
                dve.wait_ge(s_v, chain[0])

            link(nc.vector.memset(src_idx[:, :], 0))
            link(nc.vector.memset(dst_i[:, :], -1))
            assert chain[0] == V_PADS
            link(nc.vector.memset(rows_flat[:, 0:2 * LN_GROUP * IN_F], 0.0))
            link(nc.vector.memset(eps_col[:, :], EPS))
            link(nc.vector.memset(state[:, RING - 1, :], 0.0))
            link(nc.vector.memset(carry[:, :, :], 0.0))
            link(nc.vector.memset(same[:, 0:1], 0.0))
            link(nc.vector.memset(cross[:, 0:1], 0.0))
            link(nc.vector.memset(brow[:, :, :], 0.0))
            link(nc.vector.memset(x_in[:, :, :], 0.0))
            assert chain[0] == V_CLEAR

            dve.wait_ge(s_idx_in, 16 * 6)
            dve.wait_ge(s_init, 5)
            link(nc.vector.tensor_copy(src_idx[:, STEPS:STEPS + RING], src_idx[:, 0:RING]))
            for q in range(4):
                nc.vector.tensor_copy(idx_ring[:, q * QUART:(q + 1) * QUART],
                                      src_idx[:, q * QUART:(q + 1) * QUART]).then_inc(s_ring, 1)
            link(nc.vector.tensor_copy(dst_f[:, :], dst_i[:, :]))
            link(nc.vector.tensor_copy(iota_p[:, :], iota_i[:, :]))
            link(nc.vector.tensor_copy(part_base[:, :], base_i[:, :]))
            for n, c in enumerate((0, STEPS - 1)):
                link(nc.vector.tensor_copy(ends_col[:, n, :], dst_f[:, c:c + 1].to_broadcast([P, P])))
            dve.sem_inc(s_ecol)

            def ln_stats(i, b, first):
                g = 2 * i + b
                dve.wait_ge(s_x[b], 32 * (i + 1))
                for t in range(LN_GROUP):
                    ins = nc.vector.bn_stats(ln_stat[:, t, :], ln_x(b)[:, t, :])
                ins.then_inc(s_bn, 1)
                dve.wait_ge(s_bn, 2 * g + 1)
                if not (first and b == 0):
                    dve.wait_ge(s_lnsd, g)
                dve.sem_inc(s_vopen)
                for t in range(LN_GROUP):
                    ins = nc.vector.bn_aggr(ln_mv[:, t, :], ln_stat[:, t, :])
                ins.then_inc(s_lnstat, 1)
                dve.wait_ge(s_lnsd, g + 1)
                if not (first and b == 0):
                    dve.wait_ge(s_h, g)
                nc.vector.reciprocal(ln_rstd[:, :], ln_sd[:, :]).then_inc(s_bn, 1)
                dve.wait_ge(s_bn, 2 * g + 2)
                nc.vector.scalar_tensor_tensor(
                    out=ln_bias[:, :], in0=ln_mv[:, :, 0:1].rearrange("p t a -> p (t a)"), scalar=-1.0,
                    in1=ln_rstd[:, :], op0=ALU.mult, op1=ALU.mult).then_inc(s_lnscale, 1)

            for b in range(2):
                ln_stats(0, b, True)
            with dve.Fori(1, COLS // LN_GROUP // 2) as i:
                for b in range(2):
                    ln_stats(i, b, False)

            link(nc.vector.tensor_tensor(same[:, 1:STEPS], dst_f[:, 1:STEPS], dst_f[:, 0:STEPS - 1], ALU.is_equal))
            link(nc.vector.tensor_scalar(d_hi[:, :], dst_f[:, :], dst_f[:, 0:1], None, ALU.is_equal))
            link(nc.vector.tensor_reduce(first_cnt[:, :], d_hi[:, :], mybir.AxisListType.X, ALU.add))
            link(nc.vector.tensor_scalar(first_cnt[:, :], first_cnt[:, :], part_base[:, 0:1], -1.0, ALU.add, ALU.add))
            link(nc.vector.tensor_copy(fix_idx[:, :], first_cnt[:, :]))
            link(nc.vector.tensor_scalar(dst_i[:, :], dst_f[:, :], 1.0 / COLS, -(COLS - 1) / (2.0 * COLS), ALU.mult, ALU.add))
            link(nc.vector.tensor_copy(d_hi[:, :], dst_i[:, :]))
            link(nc.vector.scalar_tensor_tensor(out=d_lo[:, :], in0=d_hi[:, :], scalar=-float(COLS),
                                                in1=dst_f[:, :], op0=ALU.mult, op1=ALU.add))
            dve.wait_ge(s_erow, 1)
            link(nc.vector.tensor_copy(ends_row[:, :, :].rearrange("p a b -> p (a b)"), psum[5][:, 0:2 * P]))
            link(nc.vector.tensor_tensor(cross[:, 1:P], ends_row[:, 0, 1:P], ends_row[:, 1, 0:P - 1], ALU.is_equal))
            link(nc.vector.tensor_tensor(carry_m[:, :], ends_row[:, 0, :], ends_row[:, 1, :], ALU.is_equal))
            link(nc.vector.tensor_tensor(carry_m[:, :], carry_m[:, :], cross[:, :], ALU.mult))

            def recurrence(k):
                w = WIDTH[k]

                def body(i, first):
                    for q in range(4):
                        if not (first and k == 0):
                            dve.wait_ge(s_dump[q], 16 * (k * LOOPS + i))
                        for u in range(q * QUART, (q + 1) * QUART):
                            dve.wait_ge(s_row[u], 16 * (k * LOOPS + i + 1))
                            if not (first and u == 0):
                                dve.wait_ge(s_state, k * STEPS + i * RING + u)
                            nc.vector.scalar_tensor_tensor(
                                out=state[:, u, 0:w], in0=state[:, (u - 1) % RING, 0:w],
                                scalar=cols(same, i * RING + u), in1=rows[:, u, 0:w],
                                op0=ALU.mult, op1=COMBINE[k]).then_inc(s_state, 1)
                        nc.vector.tensor_copy(idx_ring[:, q * QUART:(q + 1) * QUART],
                                              cols(src_idx, (i + 1) * RING + q * QUART, QUART)).then_inc(s_ring, 1)
                        if k == MEAN1:
                            if not (first and q < 2):
                                dve.wait_ge(s_hist, 4 * i + q - 1)
                            b = q % 2
                            nc.vector.tensor_tensor(
                                hot_hi[:, b, :, :], iota_p[:, :].unsqueeze(1).to_broadcast([P, QUART, P]),
                                cols(d_hi, i * RING + q * QUART, QUART).unsqueeze(2).to_broadcast([P, QUART, P]),
                                ALU.is_equal)
                            nc.vector.tensor_tensor(
                                hot_lo[:, b, :, :], iota_p[:, 0:COLS].unsqueeze(1).to_broadcast([P, QUART, COLS]),
                                cols(d_lo, i * RING + q * QUART, QUART).unsqueeze(2).to_broadcast([P, QUART, COLS]),
                                ALU.is_equal).then_inc(s_hot, 1)

                body(0, True)
                with dve.Fori(1, LOOPS) as i:
                    body(i, False)

            def degrees():
                dve.wait_ge(s_hist, 4 * LOOPS)
                link(nc.vector.tensor_copy(deg[:, :], psum[7][:, 0:COLS]))
                nc.vector.tensor_tensor_scan(deg_cum[:, :], ones[:, 0:COLS], deg[:, :], 0.0,
                                             ALU.mult, ALU.add).then_inc(s_dtot, 1)
                link(nc.vector.tensor_scalar(has_in[:, :], deg[:, :], 0.5, None, ALU.is_gt))
                link(nc.vector.tensor_scalar(deg_tmp[:, :], deg[:, :], 1.0, None, ALU.max))
                link(nc.vector.reciprocal(r_mean[:, :], deg_tmp[:, :]))
                link(nc.vector.tensor_scalar(deg_tmp[:, :], deg[:, :], 1.0, None, ALU.add))
                link(nc.vector.reciprocal(r_gcn[:, :], deg_tmp[:, :]))
                dve.wait_ge(s_doff, 1)
                link(nc.vector.tensor_copy(deg_off[:, :], psum[6][:, 0:1]))
                link(nc.vector.tensor_scalar(deg_cum[:, :], deg_cum[:, :], deg_off[:, 0:1],
                                             -1.0 - PAD_E, ALU.add, ALU.add))
                link(nc.vector.tensor_tensor(deg_cum[:, :], deg_cum[:, :], has_in[:, :], ALU.mult))
                link(nc.vector.tensor_scalar(deg_cum[:, :], deg_cum[:, :], float(PAD_E), None, ALU.add))
                link(nc.vector.tensor_copy(end_idx[:, 0:COLS], deg_cum[:, :]))
                link(nc.vector.tensor_copy(end_idx[:, COLS:COLS + ENDS], end_idx[:, 0:ENDS]))
                for r in range(ENDS):
                    nc.vector.tensor_copy(end_ring[:, r:r + 1], end_idx[:, r:r + 1]).then_inc(s_eidx, 1)
                dve.sem_inc(s_deg)

            def fix_boundaries(k):
                w = WIDTH[k]
                dve.wait_ge(s_fixT, k + 1)
                for c in range(w // P):
                    ins = nc.vector.tensor_tensor_scan(tails[:, c, :], carry_m[:, :], psum[4][:, c * P:(c + 1) * P],
                                                       0.0, ALU.mult, COMBINE[k])
                link(ins)
                for c in range(w // P):
                    ins = nc.vector.tensor_tensor(carry[:, c, 1:P], tails[:, c, 0:P - 1], cross[:, 1:P], ALU.mult)
                ins.then_inc(s_carry, 1)
                dve.wait_ge(s_carryT, k + 1)
                dve.wait_ge(s_fixin, 16 * (k + 1))
                nc.vector.tensor_tensor(fix_out[:, 0:w], fix_row[:, 0:w], psum[5][:, 0:w],
                                        COMBINE[k]).then_inc(s_fixout, 1)

            def refill(k, t, r):
                nc.vector.tensor_copy(end_ring[:, r:r + 1], cols(end_idx, t + ENDS)).then_inc(s_eidx, 1)

            def finish_products(k):
                base = (k - MEAN1) * COLS

                def before(i, n, first):
                    t, s, r = i * 2 * ENDS + n, n % 2, n % ENDS
                    dve.wait_ge(s_ein[r], ein_value(k, i, n))
                    if k == MEAN1:
                        if not first:
                            dve.wait_ge(s_tT, t - 1)
                            dve.wait_ge(s_mst[s], 8 * (t - s))
                        nc.vector.tensor_scalar(scaled[:, s, 0:IN_F], ends[:, r, 0:IN_F],
                                                cols(r_mean, t), None, ALU.mult).then_inc(s_sc, 1)
                        dve.wait_ge(s_sc, t + 1)
                    else:
                        dve.wait_ge(s_tT, base + t + 1)
                    refill(k, t, r)

                def after(t, s, first):
                    dve.wait_ge(s_tmm, base + t + 1)
                    dve.wait_ge(s_add[s], (k * COLS // 2) * 16 + 8 * (t - s) + 16)
                    if not first:
                        dve.wait_ge(s_tst[s], (k * COLS // 2) * 16 + 8 * (t - s))
                    nc.vector.tensor_tensor(done[:, s, :], psum[6 + s][:, :], add_in[:, s, :],
                                            ALU.add).then_inc(s_sum, 1)

                def body(i, first):
                    for t in range(2 * ENDS):
                        before(i, t, first and t < 2)
                        if not (first and t == 0):
                            after(i * 2 * ENDS + t - 1, (t - 1) % 2, first and t < 3)

                body(0, True)
                with dve.Fori(1, COLS // (2 * ENDS)) as i:
                    body(i, False)
                after(COLS - 1, 1, False)

            def finish_sums(k):
                def tile(i, n, first):
                    t, s, r = i * 2 * ENDS + n, n % 2, n % ENDS
                    dve.wait_ge(s_ein[r], ein_value(k, i, n))
                    if k == GCN3:
                        dve.wait_ge(s_add[s], COLS * 16 + 8 * (t - s) + 16)
                        if not first:
                            dve.wait_ge(s_tst[s], COLS * 16 + 16 * (t - s))
                        nc.vector.tensor_tensor(scaled[:, s, :], ends[:, r, :], add_in[:, s, :],
                                                ALU.add).then_inc(s_sc, 1)
                        dve.wait_ge(s_sc, COLS + t + 1)
                        nc.vector.scalar_tensor_tensor(
                            out=done[:, s, :], in0=scaled[:, s, :], scalar=cols(r_gcn, t), in1=bias_v[:, :],
                            op0=ALU.mult, op1=ALU.add).then_inc(s_sum, 1)
                        refill(k, t, r)
                    else:
                        dve.wait_ge(s_add[s], 3 * COLS // 2 * 16 + 16 * (t - s) + 32)
                        nc.vector.scalar_tensor_tensor(
                            out=scaled[:, s, 0:IN_F], in0=ends[:, r, 0:IN_F], scalar=cols(r_mean, t),
                            in1=add_in[:, s, 0:IN_F], op0=ALU.mult, op1=ALU.add).then_inc(s_sc, 1)
                        dve.wait_ge(s_sc, 2 * COLS + t + 1)
                        if not first:
                            dve.wait_ge(s_out[s], 8 * (t - s))
                        nc.vector.tensor_tensor(done[:, s, 0:IN_F], scaled[:, s, 0:IN_F], x_in[:, s, :],
                                                ALU.add).then_inc(s_sum, 1)
                        refill(k, t, r)

                def body(i, first):
                    for t in range(2 * ENDS):
                        tile(i, t, first and t < 2)

                body(0, True)
                with dve.Fori(1, COLS // (2 * ENDS)) as i:
                    body(i, False)

            recurrence(MEAN1)
            degrees()
            fix_boundaries(MEAN1)
            finish_products(MEAN1)
            recurrence(POOL2)
            fix_boundaries(POOL2)
            finish_products(POOL2)
            dve.wait_ge(s_woc, N_OUT + 4)
            recurrence(GCN3)
            fix_boundaries(GCN3)
            finish_sums(GCN3)
            recurrence(MEAN4)
            fix_boundaries(MEAN4)
            finish_sums(MEAN4)


_WEIGHTS = ["W1_self", "W1_neigh", "b1", "W2_pool", "b2_pool", "W2_self", "W2_neigh", "b2",
            "W3_neigh", "b3", "W4_self", "W4_neigh", "b4", "W_fc", "b_fc"]
_INS = ["x", "src", "dst"] + [f"L0_gnn_{n}" for n in _WEIGHTS]


def kernel(**inputs):
    import numpy as _np
    import concourse.bacc as _bacc
    from concourse import mybir as _mybir
    from concourse.bass_utils import run_bass_kernel_spmd as _run

    nc = _bacc.Bacc("TRN2", target_bir_lowering=False, num_devices=1)
    arrays, args = {}, []
    for name in _INS:
        a = _np.ascontiguousarray(inputs[name])
        arrays[f"in_{name}_dram"] = a
        args.append(nc.dram_tensor(f"in_{name}_dram", a.shape, _mybir.dt.from_np(a.dtype), kind="ExternalInput").ap())
    args.append(nc.dram_tensor("out_0_dram", (N, IN_F), F32, kind="ExternalOutput").ap())
    gnn(nc, *args)
    r = _run(nc, [arrays], core_ids=[0])
    return r.results[0]["out_0_dram"]
```
